# Optimizing a Trainium2 kernel written in Bass

```python
import numpy as np
import jax
import jax.numpy as jnp

def _softmax(x, axis=-1):
    return jax.nn.softmax(x, axis=axis)

def _gelu(x):
    return jax.nn.gelu(x, approximate=True)

def _silu(x):
    return jax.nn.silu(x)

def _sigmoid(x):
    return jax.nn.sigmoid(x)

def _layernorm(x, axis=-1, eps=1e-05):
    m = jnp.mean(x, axis=axis, keepdims=True)
    v = jnp.var(x, axis=axis, keepdims=True)
    return (x - m) / jnp.sqrt(v + eps)

def _scatter_add(tgt, idx, src, axis=0):
    return tgt.at[idx].add(src)

def _segment_sum(src, seg, n):
    return jax.ops.segment_sum(src, seg, n)
kernel_name = 'mk_adj_resnorm_d1_adj_r2_06f33a'

def setup_inputs(seed: int=0):
    np.random.seed(seed)
    _w = jnp.asarray

    def _rec_inputs():
        import jax
        import jax.numpy as jnp
        _gk = jax.random.key(seed)
        x = -0.0002928 + 1 * jax.random.normal(jax.random.fold_in(_gk, 1), (8192, 256), jnp.float32)
        _w = (1.0 + jnp.arange(8192, dtype=jnp.float32)) ** (-0.5)
        _w = _w / _w.mean()
        _pij = jnp.clip(0.00195312 * _w[:, None] * _w[None, :], 0.0, 1.0)
        _a = jax.random.uniform(jax.random.fold_in(_gk, 2), (8192, 8192)) < _pij
        adj = _a.astype(jnp.int32)
        return (x, adj)
    x, adj = _rec_inputs()

    def _L0_gnn_setup():
        import jax, jax.numpy as jnp
        import numpy as np
        N = 4096
        D = 256
        key = jax.random.key(seed)
        k1, k2, k3 = jax.random.split(key, 3)
        x = jax.random.normal(k1, (N, D), dtype=jnp.float32)
        adj = jax.random.randint(k2, (N, N), 0, 2, dtype=jnp.int32)
        U = jax.random.normal(k3, (D, D), dtype=jnp.float32)
        return {'x': x, 'adj': adj, 'U': U}
    _L0_gnn_all = _L0_gnn_setup()
    _L0_gnn_in = {k: v for k, v in _L0_gnn_all.items() if k in ('U',)}
    del _L0_gnn_all
    return {'x': x, 'adj': adj, 'L0_gnn_U': _L0_gnn_in['U']}

def reference(x, adj, L0_gnn_U):
    import jax
    import jax.numpy as jnp

    def _L0_gnn_ref(x, adj, U):
        import jax, jax.numpy as jnp
        import numpy as np
        N = 4096
        D = 256
        a = adj.astype(jnp.float32)
        deg = jnp.sum(a, axis=0)
        agg = jnp.einsum('ji,jd->id', a, x) / deg[:, None]
        return jax.nn.relu(jnp.einsum('id,kd->ik', agg, U))
    x = _layernorm(x + _L0_gnn_ref(x, adj, L0_gnn_U), axis=-1)
    return x

_drawn_inputs = setup_inputs


def setup_inputs(seed=0):
    import zlib

    import numpy as np

    out = dict(_drawn_inputs(seed))
    spreads = {}
    factors = {}
    for name, (base, spread) in spreads.items():
        noise = np.random.default_rng([zlib.crc32(name.encode()), seed]).standard_normal(out[name].shape)
        drawn = base * np.exp(spread * noise) if base else spread * noise
        out[name] = jnp.asarray(drawn.astype(out[name].dtype))
    for name, factor in factors.items():
        out[name] = (out[name] * factor).astype(out[name].dtype)
    return out
```

```python
import concourse.bass as bass
from concourse import mybir
from contextlib import ExitStack


def build_graph_norm(nc, x, x_t, adj, u_t, out):
    fp32 = mybir.dt.float32
    fp32r = mybir.dt.float32r
    int32 = mybir.dt.int32
    ALU = mybir.AluOpType
    ACT = mybir.ActivationFunctionType

    P = 128
    N, D = x.shape
    EPS = 1e-5
    BANKS = 8
    DH = D // P
    GROUPS = N // (BANKS * P)
    WIDTH = BANKS * P
    PAIR = 2
    SLOTS = N // (P * PAIR)
    RING = 4
    STEPS = SLOTS // RING
    BATCHES = N // (P * PAIR)
    TILE_STEPS = 5
    assert STEPS == BANKS

    adj_slots = adj.rearrange("(s j p) (g c) -> g s p j c", p=P, j=PAIR, c=WIDTH)
    x_t_batches = x_t.rearrange("(h p) (m c) -> m p h c", p=P, c=PAIR * P)
    u_t_halves = u_t.rearrange("(h p) k -> p h k", p=P)
    x_tiles = x.rearrange("(t p) d -> t p d", p=P)
    out_tiles = out.rearrange("(t p) d -> t p d", p=P)

    ctx = ExitStack()
    with ctx:
        def sbuf(name, shape, dt):
            return ctx.enter_context(nc.sbuf_tensor(name, shape, dt))

        def sem(name):
            return ctx.enter_context(nc.semaphore(name))

        y_parts = sbuf("y_parts", [P, N // P, 2 * D], fp32r)
        adj_raw = [sbuf(f"adj_raw{r}", [P, PAIR, WIDTH], int32) for r in range(RING)]
        adj_f = [sbuf(f"adj_f{r}", [P, PAIR, WIDTH], fp32r) for r in range(RING)]
        deg_part = sbuf("deg_part", [P, WIDTH], fp32)
        u_sb = deg_part[:, 0:DH * D].rearrange("p (h k) -> p h k", h=DH)
        rows = sbuf("rows", [P, BANKS, D], fp32)
        x_t_sb = rows[:, :, :].rearrange("p b d -> p (b d)").rearrange(
            "p (r h c) -> p r h c", r=RING, h=DH)
        x_res = sbuf("x_res", [P, 2, D], fp32)
        ones = sbuf("ones", [P, 1], fp32)
        eps = sbuf("eps", [P, 1], fp32)
        rdeg = sbuf("rdeg", [P, BANKS], fp32)
        row_sum = sbuf("row_sum", [P, 1], fp32)
        neg_mean = sbuf("neg_mean", [P, 1], fp32)
        sum_sq = sbuf("sum_sq", [P, 1], fp32)
        std = sbuf("std", [P, 1], fp32)
        rstd = sbuf("rstd", [P, 1], fp32)
        acc = [ctx.enter_context(nc.psum_tensor(f"acc{b}", [P, 2 * D], fp32)) for b in range(BANKS)]

        u_loaded = sem("u_loaded")
        x_t_loaded = [sem(f"x_t_loaded{r}") for r in range(RING)]
        y_summed = sem("y_summed")
        y_high_done = sem("y_high_done")
        bank_free = sem("bank_free")
        adj_loaded = [sem(f"adj_loaded{r}") for r in range(RING)]
        adj_converted = sem("adj_converted")
        adj_counted = sem("adj_counted")
        deg_cleared = sem("deg_cleared")
        banks_summed = sem("banks_summed")
        high_copied = sem("high_copied")
        deg_summed = sem("deg_summed")
        rdeg_ready = sem("rdeg_ready")
        consts_ready = sem("consts_ready")
        x_res_loaded = [sem(f"x_res_loaded{k}") for k in range(2)]
        tile_step = sem("tile_step")
        squares_summed = sem("squares_summed")
        std_ready = sem("std_ready")
        stored = sem("stored")

        block = ctx.enter_context(nc.Block())

        @block.gpsimd
        def _(pool):
            nc.gpsimd.memset(ones[:, :], 1.0).then_inc(consts_ready, 1)
            nc.gpsimd.memset(eps[:, :], EPS).then_inc(consts_ready, 1)

        @block.sync
        def _(sp):
            sp.dma_start(u_sb, u_t_halves).then_inc(u_loaded, 16)
            for r in range(RING):
                sp.dma_start(x_t_sb[:, r], x_t_batches[r]).then_inc(x_t_loaded[r], 16)
            with sp.Fori(1, BATCHES // RING) as q:
                for r in range(RING):
                    sp.wait_ge(y_summed, q * RING + (r - RING + 1))
                    sp.dma_start(x_t_sb[:, r], x_t_batches[q * RING + r]).then_inc(x_t_loaded[r], 16)

            def load_adj(g, s, r):
                n = g * SLOTS + s
                sp.wait_ge(adj_converted, n + (1 - RING))
                sp.wait_ge(adj_counted, PAIR * n + PAIR * (1 - RING))
                sp.dma_start(adj_raw[r][:, :, :], adj_slots[g, s]).then_inc(adj_loaded[r], 16)

            def load_x_res(tile, k):
                sp.dma_start(x_res[:, k], x_tiles[tile]).then_inc(x_res_loaded[k], 16)

            def store(tile, b):
                sp.wait_ge(tile_step, TILE_STEPS * tile + TILE_STEPS)
                sp.dma_start(out_tiles[tile], rows[:, b]).then_inc(stored, 16)

            for r in range(RING):
                sp.dma_start(adj_raw[r][:, :, :], adj_slots[0, r]).then_inc(adj_loaded[r], 16)
            for s in range(2):
                load_x_res(s, s)
            with sp.Fori(0, STEPS - 1) as i:
                for r in range(RING):
                    load_adj(0, i * RING + (RING + r), r)
            for r in range(RING):
                load_adj(1, r, r)

            def group_loads(g, last):
                first_tile = (g - 1) * BANKS

                def finish_tile(b, k):
                    store(first_tile + b, b)
                    load_x_res(first_tile + b + 2, k)

                with sp.Fori(0, STEPS // 2 - 1) as i:
                    for k in range(2):
                        for r in range(RING):
                            load_adj(g, i * (2 * RING) + (k * RING + RING + r), r)
                        finish_tile(i * 2 + k, k)
                for r in range(RING):
                    load_adj(g, (STEPS - 1) * RING + r, r)
                finish_tile(STEPS - 2, 0)
                if not last:
                    for r in range(RING):
                        load_adj(g + 1, r, r)
                finish_tile(STEPS - 1, 1)

            with sp.Fori(1, GROUPS - 1) as g:
                group_loads(g, False)
            group_loads(GROUPS - 1, True)

            for b in range(BANKS):
                tile = (GROUPS - 1) * BANKS + b
                store(tile, b)
                if b + 2 < BANKS:
                    load_x_res(tile + 2, b % 2)
            sp.wait_ge(stored, 16 * GROUPS * BANKS)

        @block.tensor
        def _(pe):
            pe.wait_ge(u_loaded, 16)

            def project(q, r, k, wait_bank):
                pe.wait_ge(x_t_loaded[r], 16 * q + 16)
                if wait_bank:
                    pe.wait_ge(bank_free, q * RING + (r - BANKS + 1))
                for j in range(PAIR):
                    for h in range(DH):
                        done = nc.tensor.matmul(acc[k][:, j * D:(j + 1) * D], x_t_sb[:, r, h, j * P:(j + 1) * P],
                                                u_sb[:, h], start=(h == 0), stop=(h == DH - 1))
                done.then_inc(y_summed, 1)

            for q in range(2):
                for r in range(RING):
                    project(q, r, q * RING + r, False)
            with pe.Fori(1, BATCHES // BANKS) as i:
                for q in range(2):
                    for r in range(RING):
                        project(i * 2 + q, r, q * RING + r, True)

            pe.wait_ge(consts_ready, 2)

            def sum_slot(g, s, r, first):
                pe.wait_ge(adj_converted, g * SLOTS + s + 1)
                moving = [y_parts[:, bass.ds(s * PAIR + j, 1), :].rearrange("p o n -> p (o n)") for j in range(PAIR)]
                for b in ([*range(1, BANKS), 0] if first else range(BANKS)):
                    if first:
                        pe.wait_ge(bank_free, g * BANKS + (BATCHES - BANKS + b + 1))
                        if b == 0:
                            pe.wait_ge(deg_cleared, g + 1)
                    for j in range(PAIR):
                        done = nc.tensor.matmul(acc[b][:, :], adj_f[r][:, j, b * P:(b + 1) * P], moving[j],
                                                start=(first and j == 0), stop=False, skip_group_check=True)
                    done.then_inc(banks_summed, 1)

            with pe.Fori(0, GROUPS) as g:
                for r in range(RING):
                    sum_slot(g, r, r, r == 0)
                with pe.Fori(1, STEPS) as i:
                    for r in range(RING):
                        sum_slot(g, i * RING + r, r, False)
                pe.wait_ge(adj_counted, g * (SLOTS * PAIR) + SLOTS * PAIR)
                pe.wait_ge(bank_free, g * BANKS + (BATCHES + 1))
                for b in range(BANKS):
                    done = nc.tensor.matmul(acc[0][:, b:b + 1], deg_part[:, b * P:(b + 1) * P], ones[:, :],
                                            start=True, stop=True, skip_group_check=True)
                done.then_inc(deg_summed, 1)

        @block.scalar
        def _(act):
            with act.Fori(0, BATCHES // BANKS) as i:
                for k in range(BANKS):
                    m = i * BANKS + k
                    act.wait_ge(y_summed, m + 1)
                    high = y_parts[:, bass.ds(m * PAIR, PAIR), 0:D]
                    nc.scalar.activation(high, acc[k][:, :].rearrange("p (j d) -> p j d", j=PAIR),
                                         ACT.Copy).then_inc(y_high_done, 1)

            def convert(n, q, r, wait_used=True):
                act.wait_ge(adj_loaded[r], 16 * q + 16)
                if wait_used:
                    act.wait_ge(banks_summed, BANKS * n + BANKS * (1 - RING))
                nc.scalar.activation(adj_f[r][:, :, :], adj_raw[r][:, :, :], ACT.Copy).then_inc(adj_converted, 1)

            def find_std(tile, b, k):
                act.wait_ge(tile_step, TILE_STEPS * tile + 3)
                nc.scalar.activation(x_res[:, k], rows[:, b], ACT.Square, bias=neg_mean[:, :],
                                     accum_out=sum_sq[:, :]).then_inc(squares_summed, 1)
                act.wait_ge(squares_summed, tile + 1)
                nc.scalar.activation(std[:, :], sum_sq[:, :], ACT.Sqrt, bias=eps[:, :], scale=1.0 / D).then_inc(std_ready, 1)

            def convert_step(g, i, k=None):
                q = g * STEPS + i
                convert(q * RING + 2, q, 2)
                convert(q * RING + 3, q, 3)
                if k is not None:
                    find_std((g - 1) * BANKS + i, bass.ds(i, 1), k)
                convert(q * RING + 4, q + 1, 0)
                convert(q * RING + 5, q + 1, 1)

            def copy_high_halves(g, wait_stored=True):
                if wait_stored:
                    act.wait_ge(stored, g * (16 * BANKS))
                for b in range(BANKS):
                    act.wait_ge(banks_summed, g * (SLOTS * BANKS) + ((SLOTS - 1) * BANKS + b + 1))
                    nc.scalar.activation(rows[:, b], acc[b][:, 0:D], ACT.Copy).then_inc(high_copied, 1)

            act.wait_ge(consts_ready, 2)
            convert(0, 0, 0, False)
            convert(1, 0, 1, False)
            convert(2, 0, 2, False)
            convert(3, 0, 3, False)
            convert(4, 1, 0)
            convert(5, 1, 1)
            with act.Fori(1, STEPS) as i:
                convert_step(0, i)
            copy_high_halves(0, False)
            with act.Fori(1, GROUPS - 1) as g:
                with act.Fori(0, STEPS // 2) as i:
                    for k in range(2):
                        convert_step(g, i * 2 + k, k)
                copy_high_halves(g)
            last = GROUPS - 1
            with act.Fori(0, STEPS // 2 - 1) as i:
                for k in range(2):
                    convert_step(last, i * 2 + k, k)
            convert_step(last, STEPS - 2, 0)
            q = GROUPS * STEPS - 1
            convert(q * RING + 2, q, 2)
            convert(q * RING + 3, q, 3)
            find_std(last * BANKS - 1, slice(BANKS - 1, BANKS), 1)
            copy_high_halves(last)
            for b in range(BANKS):
                find_std(last * BANKS + b, slice(b, b + 1), b % 2)

        @block.vector
        def _(dve):
            with dve.Fori(0, BATCHES // BANKS) as i:
                for k in range(BANKS):
                    m = i * BANKS + k
                    dve.wait_ge(y_high_done, m + 1)
                    high = y_parts[:, bass.ds(m * PAIR, PAIR), 0:D].bitcast(fp32)
                    low = y_parts[:, bass.ds(m * PAIR, PAIR), D:2 * D]
                    nc.vector.tensor_tensor(low, acc[k][:, :].rearrange("p (j d) -> p j d", j=PAIR), high,
                                            ALU.subtract).then_inc(bank_free, 1)

            def clear_deg(g):
                nc.vector.memset(deg_part[:, :], 0.0).then_inc(deg_cleared, 1)

            def count_slot(n, q, r, g=None, first=False):
                if g is not None:
                    dve.wait_ge(deg_cleared, g + 1)
                dve.wait_ge(adj_loaded[r], 16 * q + 16)
                for j in range(PAIR):
                    if not first or r or j:
                        dve.wait_ge(adj_counted, n * PAIR + j)
                    nc.vector.tensor_tensor(deg_part[:, :], deg_part[:, :], adj_raw[r][:, j], ALU.add).then_inc(adj_counted, 1)

            def scale_and_add_x(tile, b, k, q, g):
                dve.wait_ge(rdeg_ready, g + 1)
                nc.vector.tensor_scalar(rows[:, b], rows[:, b], 0.0, rdeg[:, b], ALU.max, ALU.mult).then_inc(tile_step, 1)
                dve.wait_ge(tile_step, TILE_STEPS * tile + 1)
                dve.wait_ge(x_res_loaded[k], 16 * q + 16)
                nc.vector.scalar_tensor_tensor(rows[:, b], rows[:, b], 1.0, x_res[:, k:k + 1], ALU.mult, ALU.add,
                                               accum_out=row_sum[:, :]).then_inc(tile_step, 1)

            def find_neg_mean(tile):
                dve.wait_ge(tile_step, TILE_STEPS * tile + 2)
                nc.vector.tensor_scalar(neg_mean[:, :], row_sum[:, :], -1.0 / D, None, ALU.mult).then_inc(tile_step, 1)

            def normalise(tile, b):
                dve.wait_ge(std_ready, tile + 1)
                nc.vector.reciprocal(rstd[:, :], std[:, :]).then_inc(tile_step, 1)
                dve.wait_ge(tile_step, TILE_STEPS * tile + 4)
                nc.vector.tensor_scalar(rows[:, b], rows[:, b], neg_mean[:, :], rstd[:, :],
                                        ALU.add, ALU.mult).then_inc(tile_step, 1)

            def empty_banks(g):
                for b in range(BANKS):
                    dve.wait_ge(high_copied, g * BANKS + (b + 1))
                    nc.vector.tensor_tensor(rows[:, b], acc[b][:, D:2 * D], rows[:, b], ALU.add).then_inc(bank_free, 1)
                dve.wait_ge(deg_summed, g + 1)
                nc.vector.reciprocal(rdeg[:, :], acc[0][:, 0:BANKS]).then_inc(rdeg_ready, 1)

            clear_deg(0)
            for r in range(RING):
                count_slot(r, 0, r, 0 if r == 0 else None, first=True)
            with dve.Fori(1, STEPS) as i:
                for r in range(RING):
                    count_slot(i * RING + r, i, r, 0 if r == 0 else None)
            empty_banks(0)
            with dve.Fori(1, GROUPS) as g:
                clear_deg(g)
                with dve.Fori(0, STEPS // 2) as i:
                    for k in range(2):
                        q = g * STEPS + i * 2 + k
                        b = bass.ds(i * 2 + k, 1)
                        tile = (g - 1) * BANKS + i * 2 + k
                        count_slot(q * RING, q, 0, g)
                        scale_and_add_x(tile, b, k, (g - 1) * (BANKS // 2) + i, g - 1)
                        count_slot(q * RING + 1, q, 1)
                        find_neg_mean(tile)
                        count_slot(q * RING + 2, q, 2)
                        count_slot(q * RING + 3, q, 3)
                        normalise(tile, b)
                empty_banks(g)
            for b in range(BANKS):
                tile = (GROUPS - 1) * BANKS + b
                scale_and_add_x(tile, slice(b, b + 1), b % 2, tile // 2, GROUPS - 1)
                find_neg_mean(tile)
                normalise(tile, slice(b, b + 1))


def kernel(x, adj, L0_gnn_U):
    import numpy as np
    import concourse.bacc as bacc
    from concourse.bass_utils import run_bass_kernel_spmd

    x, adj, u = np.asarray(x), np.asarray(adj), np.asarray(L0_gnn_U)
    arrays = {
        "x": np.ascontiguousarray(x),
        "x_t": np.ascontiguousarray(x.T),
        "adj": np.ascontiguousarray(adj),
        "u_t": np.ascontiguousarray(u.T),
    }
    nc = bacc.Bacc("TRN2", target_bir_lowering=False, num_devices=1)
    args = [nc.dram_tensor(name, a.shape, mybir.dt.from_np(a.dtype), kind="ExternalInput").ap()
            for name, a in arrays.items()]
    out = nc.dram_tensor("out", x.shape, mybir.dt.float32, kind="ExternalOutput").ap()
    build_graph_norm(nc, *args, out)
    return run_bass_kernel_spmd(nc, [arrays], core_ids=[0]).results[0]["out"]
```

```python
import concourse.bass as bass
from concourse import mybir
from contextlib import ExitStack


def build_graph_norm(nc, x, x_t, adj, u_t, out):
    fp32 = mybir.dt.float32
    fp32r = mybir.dt.float32r
    int32 = mybir.dt.int32
    ALU = mybir.AluOpType
    ACT = mybir.ActivationFunctionType

    P = 128
    N, D = x.shape
    EPS = 1e-5
    BANKS = 8
    DH = D // P
    GROUPS = N // (BANKS * P)
    WIDTH = BANKS * P
    PAIR = 2
    SLOTS = N // (P * PAIR)
    RING = 4
    STEPS = SLOTS // RING
    LAST = GROUPS - 1
    BATCHES = N // (P * PAIR)
    MEAN_STEPS = 3
    NORM_STEPS = 2
    DEG_AFTER = 4
    assert STEPS == BANKS

    adj_slots = adj.rearrange("(s j p) (g c) -> g s p j c", p=P, j=PAIR, c=WIDTH)
    x_t_batches = x_t.rearrange("(h p) (m c) -> m p h c", p=P, c=PAIR * P)
    u_t_halves = u_t.rearrange("(h p) k -> p h k", p=P)
    x_last_tiles = x[N - WIDTH:N, :].rearrange("(t p) d -> p t d", p=P)
    x_tiles = x.rearrange("(t p) d -> t p d", p=P)
    out_tiles = out.rearrange("(t p) d -> t p d", p=P)

    ctx = ExitStack()
    with ctx:
        def sbuf(name, shape, dt):
            return ctx.enter_context(nc.sbuf_tensor(name, shape, dt))

        def sem(name):
            return ctx.enter_context(nc.semaphore(name))

        y_parts = sbuf("y_parts", [P, N // P, 2 * D], fp32r)
        adj_raw = [sbuf(f"adj_raw{r}", [P, PAIR, WIDTH], int32) for r in range(RING)]
        adj_f = [sbuf(f"adj_f{r}", [P, PAIR, WIDTH], fp32r) for r in range(RING)]
        deg_part = sbuf("deg_part", [P, WIDTH], fp32)
        u_sb = deg_part[:, 0:DH * D].rearrange("p (h k) -> p h k", h=DH)
        rows = sbuf("rows", [P, BANKS, D], fp32)
        x_t_sb = rows[:, :, :].rearrange("p b d -> p (b d)").rearrange(
            "p (r h c) -> p r h c", r=RING, h=DH)
        x_res = sbuf("x_res", [P, 2, D], fp32)
        ones = sbuf("ones", [P, 1], fp32)
        eps = sbuf("eps", [P, 1], fp32)
        rdeg = sbuf("rdeg", [P, BANKS], fp32)
        row_sum = sbuf("row_sum", [P, 2], fp32)
        neg_mean = sbuf("neg_mean", [P, 2], fp32)
        sum_sq = sbuf("sum_sq", [P, 2], fp32)
        std = sbuf("std", [P, 2], fp32)
        rstd = sbuf("rstd", [P, 2], fp32)
        x_last = adj_raw[0][:, :, :].bitcast(fp32).rearrange(
            "p j (t d) -> p (j t) d", d=D)
        acc = [ctx.enter_context(nc.psum_tensor(f"acc{b}", [P, 2 * D], fp32)) for b in range(BANKS)]

        u_loaded = sem("u_loaded")
        x_t_loaded = [sem(f"x_t_loaded{r}") for r in range(RING)]
        y_summed = sem("y_summed")
        y_high_done = sem("y_high_done")
        bank_free = sem("bank_free")
        adj_loaded = [sem(f"adj_loaded{r}") for r in range(RING)]
        adj_converted = sem("adj_converted")
        adj_counted = sem("adj_counted")
        deg_cleared = sem("deg_cleared")
        banks_summed = sem("banks_summed")
        high_copied = sem("high_copied")
        deg_summed = sem("deg_summed")
        rdeg_ready = sem("rdeg_ready")
        consts_ready = sem("consts_ready")
        x_res_loaded = [sem(f"x_res_loaded{k}") for k in range(2)]
        x_last_loaded = sem("x_last_loaded")
        mean_step = sem("mean_step")
        norm_step = sem("norm_step")
        squares_summed = sem("squares_summed")
        std_ready = sem("std_ready")
        stored = sem("stored")

        block = ctx.enter_context(nc.Block())

        @block.gpsimd
        def _(pool):
            nc.gpsimd.memset(ones[:, :], 1.0).then_inc(consts_ready, 1)
            nc.gpsimd.memset(eps[:, :], EPS).then_inc(consts_ready, 1)

        @block.sync
        def _(sp):
            for r in range(RING):
                sp.dma_start(x_t_sb[:, r], x_t_batches[r]).then_inc(x_t_loaded[r], 16)

            def load_x_t(q, r):
                sp.wait_ge(y_summed, q * RING + (r - RING + 1))
                sp.dma_start(x_t_sb[:, r], x_t_batches[q * RING + r]).then_inc(x_t_loaded[r], 16)

            with sp.Fori(1, BATCHES // RING - RING) as q:
                for r in range(RING):
                    load_x_t(q, r)
            for k in range(RING):
                for r in range(RING):
                    load_x_t(BATCHES // RING - RING + k, r)
                sp.dma_start(adj_raw[k][:, :, :], adj_slots[0, k]).then_inc(adj_loaded[k], 16)

            def load_adj(g, s, r):
                n = g * SLOTS + s
                sp.wait_ge(adj_converted, n + (1 - RING))
                sp.wait_ge(adj_counted, PAIR * n + PAIR * (1 - RING))
                sp.dma_start(adj_raw[r][:, :, :], adj_slots[g, s]).then_inc(adj_loaded[r], 16)

            def load_x_res(tile, k):
                sp.dma_start(x_res[:, k], x_tiles[tile]).then_inc(x_res_loaded[k], 16)

            def store(tile, b):
                sp.wait_ge(norm_step, NORM_STEPS * tile + NORM_STEPS)
                sp.dma_start(out_tiles[tile], rows[:, b]).then_inc(stored, 16)

            for s in range(2):
                load_x_res(s, s)
            with sp.Fori(0, STEPS - 1) as i:
                for r in range(RING):
                    load_adj(0, i * RING + (RING + r), r)
            for r in range(RING):
                load_adj(1, r, r)

            def group_loads(g, last):
                first_tile = (g - 1) * BANKS

                def finish_tile(b, k, load=True):
                    store(first_tile + b, b)
                    if load:
                        load_x_res(first_tile + b + 2, k)

                with sp.Fori(0, STEPS // 2 - 1) as i:
                    for k in range(2):
                        for r in range(RING):
                            load_adj(g, i * (2 * RING) + (k * RING + RING + r), r)
                        finish_tile(i * 2 + k, k)
                for r in range(RING):
                    load_adj(g, (STEPS - 1) * RING + r, r)
                finish_tile(STEPS - 2, 0, not last)
                if not last:
                    for r in range(RING):
                        load_adj(g + 1, r, r)
                else:
                    n = GROUPS * SLOTS - RING
                    sp.wait_ge(adj_converted, n + 1)
                    sp.wait_ge(adj_counted, PAIR * n + PAIR)
                    sp.dma_start(x_last, x_last_tiles).then_inc(x_last_loaded, 16)
                finish_tile(STEPS - 1, 1, not last)

            with sp.Fori(1, GROUPS - 1) as g:
                group_loads(g, False)
            group_loads(LAST, True)

            for b in range(BANKS):
                store(LAST * BANKS + b, b)
            sp.wait_ge(stored, 16 * GROUPS * BANKS)

        @block.tensor
        def _(pe):
            pe.wait_ge(u_loaded, 16)

            def project(q, r, k, wait_bank):
                pe.wait_ge(x_t_loaded[r], 16 * q + 16)
                if wait_bank:
                    pe.wait_ge(bank_free, q * RING + (r - BANKS + 1))
                for j in range(PAIR):
                    for h in range(DH):
                        done = nc.tensor.matmul(acc[k][:, j * D:(j + 1) * D], x_t_sb[:, r, h, j * P:(j + 1) * P],
                                                u_sb[:, h], start=(h == 0), stop=(h == DH - 1))
                done.then_inc(y_summed, 1)

            for q in range(2):
                for r in range(RING):
                    project(q, r, q * RING + r, False)
            with pe.Fori(1, BATCHES // BANKS) as i:
                for q in range(2):
                    for r in range(RING):
                        project(i * 2 + q, r, q * RING + r, True)

            pe.wait_ge(consts_ready, 2)

            def moving(s, j):
                return y_parts[:, bass.ds(s * PAIR + j, 1), :].rearrange("p o n -> p (o n)")

            def sum_degrees(g):
                pe.wait_ge(adj_counted, g * (SLOTS * PAIR) + SLOTS * PAIR)
                pe.wait_ge(bank_free, g * BANKS + (BATCHES + 1))
                for b in range(BANKS):
                    done = nc.tensor.matmul(acc[0][:, b:b + 1], deg_part[:, b * P:(b + 1) * P], ones[:, :],
                                            start=True, stop=True, skip_group_check=True)
                done.then_inc(deg_summed, 1)

            def sum_slot(g, s, r, first=False, last=False):
                pe.wait_ge(adj_converted, g * SLOTS + s + 1)
                rhs = [moving(s, j) for j in range(PAIR)]
                for b in ([*range(1, BANKS), 0] if first else range(BANKS)):
                    if first:
                        pe.wait_ge(bank_free, g * BANKS + (BATCHES - BANKS + b + 1))
                        if b == 0:
                            pe.wait_ge(deg_cleared, g + 1)
                    for j in range(PAIR):
                        done = nc.tensor.matmul(acc[b][:, :], adj_f[r][:, j, b * P:(b + 1) * P], rhs[j],
                                                start=(first and j == 0), stop=False, skip_group_check=True)
                    done.then_inc(banks_summed, 1)
                    if last and b == DEG_AFTER:
                        sum_degrees(g)

            def sum_steps(g, steps):
                for r in range(RING):
                    sum_slot(g, r, r, first=(r == 0))
                with pe.Fori(1, steps) as i:
                    for r in range(RING):
                        sum_slot(g, i * RING + r, r)

            with pe.Fori(0, LAST) as g:
                sum_steps(g, STEPS - 1)
                for r in range(RING):
                    sum_slot(g, (STEPS - 1) * RING + r, r, last=(r == RING - 1))
            sum_steps(LAST, STEPS - 1)
            for b in range(BANKS):
                for r in range(RING):
                    s = (STEPS - 1) * RING + r
                    if b == 0:
                        pe.wait_ge(adj_converted, LAST * SLOTS + s + 1)
                    for j in range(PAIR):
                        done = nc.tensor.matmul(acc[b][:, :], adj_f[r][:, j, b * P:(b + 1) * P], moving(s, j),
                                                start=False, stop=(r == RING - 1 and j == PAIR - 1),
                                                skip_group_check=True)
                done.then_inc(banks_summed, 1)
                if b == 1:
                    sum_degrees(LAST)

        @block.scalar
        def _(act):
            act.dma_start(u_sb, u_t_halves).then_inc(u_loaded, 16)
            def write_high(i, k):
                m = i * BANKS + k
                act.wait_ge(y_summed, m + 1)
                high = y_parts[:, bass.ds(m * PAIR, PAIR), 0:D]
                nc.scalar.activation(high, acc[k][:, :].rearrange("p (j d) -> p j d", j=PAIR),
                                     ACT.Copy).then_inc(y_high_done, 1)

            def convert(n, q, r, wait_used=True):
                act.wait_ge(adj_loaded[r], 16 * q + 16)
                if wait_used:
                    act.wait_ge(banks_summed, BANKS * n + BANKS * (1 - RING))
                nc.scalar.activation(adj_f[r][:, :, :], adj_raw[r][:, :, :], ACT.Copy).then_inc(adj_converted, 1)

            def find_std(tile, b, k, last_b=None):
                act.wait_ge(mean_step, MEAN_STEPS * tile + MEAN_STEPS)
                one = slice(k, k + 1)
                scratch = x_res[:, k] if last_b is None else x_last[:, last_b]
                nc.scalar.activation(scratch, rows[:, b], ACT.Square, bias=neg_mean[:, one],
                                     accum_out=sum_sq[:, one]).then_inc(squares_summed, 1)
                act.wait_ge(squares_summed, tile + 1)
                nc.scalar.activation(std[:, one], sum_sq[:, one], ACT.Sqrt, bias=eps[:, :], scale=1.0 / D).then_inc(std_ready, 1)

            def convert_step(g, i, k=None):
                q = g * STEPS + i
                convert(q * RING + 2, q, 2)
                convert(q * RING + 3, q, 3)
                if k is not None:
                    find_std((g - 1) * BANKS + i, bass.ds(i, 1), k)
                convert(q * RING + 4, q + 1, 0)
                convert(q * RING + 5, q + 1, 1)

            def copy_high_half(before, b):
                act.wait_ge(banks_summed, before + (b + 1))
                nc.scalar.activation(rows[:, b], acc[b][:, 0:D], ACT.Copy).then_inc(high_copied, 1)

            def copy_high_halves(g, wait_stored=True):
                if wait_stored:
                    act.wait_ge(stored, g * (16 * BANKS))
                for b in range(BANKS):
                    copy_high_half(g * (SLOTS * BANKS) + (SLOTS - 1) * BANKS, b)

            with act.Fori(0, BATCHES // BANKS - 1) as i:
                for k in range(BANKS):
                    write_high(i, k)
            act.wait_ge(consts_ready, 2)
            for k in range(BANKS):
                write_high(BATCHES // BANKS - 1, k)
                if k == 2:
                    convert(0, 0, 0, False)
                if k == 5:
                    convert(1, 0, 1, False)
            convert(2, 0, 2, False)
            convert(3, 0, 3, False)
            convert(4, 1, 0)
            convert(5, 1, 1)
            with act.Fori(1, STEPS) as i:
                convert_step(0, i)
            copy_high_halves(0, False)
            with act.Fori(1, GROUPS - 1) as g:
                with act.Fori(0, STEPS // 2) as i:
                    for k in range(2):
                        convert_step(g, i * 2 + k, k)
                copy_high_halves(g)
            with act.Fori(0, STEPS // 2 - 1) as i:
                for k in range(2):
                    convert_step(LAST, i * 2 + k, k)
            convert_step(LAST, STEPS - 2, 0)
            q = GROUPS * STEPS - 1
            convert(q * RING + 2, q, 2)
            convert(q * RING + 3, q, 3)
            find_std(LAST * BANKS - 1, slice(BANKS - 1, BANKS), 1)
            act.wait_ge(stored, LAST * 16 * BANKS)
            for b in range(BANKS + 1):
                if b < BANKS:
                    copy_high_half((GROUPS * SLOTS - RING) * BANKS, b)
                if b >= 1:
                    find_std(LAST * BANKS + b - 1, slice(b - 1, b), (b - 1) % 2, b - 1)

        @block.vector
        def _(dve):
            with dve.Fori(0, BATCHES // BANKS) as i:
                for k in range(BANKS):
                    m = i * BANKS + k
                    dve.wait_ge(y_high_done, m + 1)
                    high = y_parts[:, bass.ds(m * PAIR, PAIR), 0:D].bitcast(fp32)
                    low = y_parts[:, bass.ds(m * PAIR, PAIR), D:2 * D]
                    nc.vector.tensor_tensor(low, acc[k][:, :].rearrange("p (j d) -> p j d", j=PAIR), high,
                                            ALU.subtract).then_inc(bank_free, 1)

            def clear_deg(g):
                nc.vector.memset(deg_part[:, :], 0.0).then_inc(deg_cleared, 1)

            def count_slot(n, q, r, g=None, first=False):
                if g is not None:
                    dve.wait_ge(deg_cleared, g + 1)
                dve.wait_ge(adj_loaded[r], 16 * q + 16)
                for j in range(PAIR):
                    if not first or r or j:
                        dve.wait_ge(adj_counted, n * PAIR + j)
                    nc.vector.tensor_tensor(deg_part[:, :], deg_part[:, :], adj_raw[r][:, j], ALU.add).then_inc(adj_counted, 1)

            def scale_and_add_x(tile, b, k, g, x_tile):
                dve.wait_ge(rdeg_ready, g + 1)
                dve.wait_ge(bank_free, tile + (BATCHES + 1))
                nc.vector.tensor_scalar(rows[:, b], rows[:, b], 0.0, rdeg[:, b], ALU.max, ALU.mult).then_inc(mean_step, 1)
                dve.wait_ge(mean_step, MEAN_STEPS * tile + 1)
                nc.vector.scalar_tensor_tensor(rows[:, b], rows[:, b], 1.0, x_tile, ALU.mult, ALU.add,
                                               accum_out=row_sum[:, k:k + 1]).then_inc(mean_step, 1)

            def find_neg_mean(tile, k):
                dve.wait_ge(mean_step, MEAN_STEPS * tile + 2)
                nc.vector.tensor_scalar(neg_mean[:, k:k + 1], row_sum[:, k:k + 1], -1.0 / D, None,
                                        ALU.mult).then_inc(mean_step, 1)

            def normalise(tile, b, k):
                dve.wait_ge(std_ready, tile + 1)
                nc.vector.reciprocal(rstd[:, k:k + 1], std[:, k:k + 1]).then_inc(norm_step, 1)
                dve.wait_ge(norm_step, NORM_STEPS * tile + 1)
                nc.vector.tensor_scalar(rows[:, b], rows[:, b], neg_mean[:, k:k + 1], rstd[:, k:k + 1],
                                        ALU.add, ALU.mult).then_inc(norm_step, 1)

            def add_low_half(g, b):
                dve.wait_ge(high_copied, g * BANKS + (b + 1))
                nc.vector.tensor_tensor(rows[:, b], acc[b][:, D:2 * D], rows[:, b], ALU.add).then_inc(bank_free, 1)

            def invert_degrees(g):
                dve.wait_ge(deg_summed, g + 1)
                nc.vector.reciprocal(rdeg[:, :], acc[0][:, 0:BANKS]).then_inc(rdeg_ready, 1)

            def empty_banks(g):
                for b in range(BANKS):
                    add_low_half(g, b)
                    if b == DEG_AFTER + 1:
                        invert_degrees(g)

            clear_deg(0)
            for r in range(RING):
                count_slot(r, 0, r, 0 if r == 0 else None, first=True)
            with dve.Fori(1, STEPS) as i:
                for r in range(RING):
                    count_slot(i * RING + r, i, r, 0 if r == 0 else None)
            empty_banks(0)

            def group(g):
                clear_deg(g)
                with dve.Fori(0, STEPS // 2) as i:
                    for k in range(2):
                        q = g * STEPS + i * 2 + k
                        b = bass.ds(i * 2 + k, 1)
                        tile = (g - 1) * BANKS + i * 2 + k
                        count_slot(q * RING, q, 0, g)
                        dve.wait_ge(x_res_loaded[k], (g - 1) * (16 * BANKS // 2) + (i * 16 + 16))
                        scale_and_add_x(tile, b, k, g - 1, x_res[:, k:k + 1])
                        count_slot(q * RING + 1, q, 1)
                        find_neg_mean(tile, k)
                        count_slot(q * RING + 2, q, 2)
                        count_slot(q * RING + 3, q, 3)
                        normalise(tile, b, k)

            with dve.Fori(1, LAST) as g:
                group(g)
                empty_banks(g)
            group(LAST)

            def last_tile(b):
                add_low_half(LAST, b)
                scale_and_add_x(LAST * BANKS + b, slice(b, b + 1), b % 2, LAST, x_last[:, b:b + 1])
                find_neg_mean(LAST * BANKS + b, b % 2)

            add_low_half(LAST, 0)
            invert_degrees(LAST)
            dve.wait_ge(x_last_loaded, 16)
            scale_and_add_x(LAST * BANKS, slice(0, 1), 0, LAST, x_last[:, 0:1])
            find_neg_mean(LAST * BANKS, 0)
            for b in range(1, BANKS):
                last_tile(b)
                normalise(LAST * BANKS + b - 1, slice(b - 1, b), (b - 1) % 2)
            normalise(LAST * BANKS + BANKS - 1, slice(BANKS - 1, BANKS), (BANKS - 1) % 2)


def kernel(x, adj, L0_gnn_U):
    import numpy as np
    import concourse.bacc as bacc
    from concourse.bass_utils import run_bass_kernel_spmd

    x, adj, u = np.asarray(x), np.asarray(adj), np.asarray(L0_gnn_U)
    arrays = {
        "x": np.ascontiguousarray(x),
        "x_t": np.ascontiguousarray(x.T),
        "adj": np.ascontiguousarray(adj),
        "u_t": np.ascontiguousarray(u.T),
    }
    nc = bacc.Bacc("TRN2", target_bir_lowering=False, num_devices=1)
    args = [nc.dram_tensor(name, a.shape, mybir.dt.from_np(a.dtype), kind="ExternalInput").ap()
            for name, a in arrays.items()]
    out = nc.dram_tensor("out", x.shape, mybir.dt.float32, kind="ExternalOutput").ap()
    build_graph_norm(nc, *args, out)
    return run_bass_kernel_spmd(nc, [arrays], core_ids=[0]).results[0]["out"]
```

```python
import concourse.bass as bass
from concourse import mybir
from contextlib import ExitStack


def build_graph_norm(nc, x, x_t, adj, u_t, out):
    fp32 = mybir.dt.float32
    fp32r = mybir.dt.float32r
    int32 = mybir.dt.int32
    ALU = mybir.AluOpType
    ACT = mybir.ActivationFunctionType

    P = 128
    N, D = x.shape
    EPS = 1e-5
    BANKS = 8
    DH = D // P
    GROUPS = N // (BANKS * P)
    WIDTH = BANKS * P
    PAIR = 2
    SLOTS = N // (P * PAIR)
    RING = 4
    STEPS = SLOTS // RING
    LAST = GROUPS - 1
    BATCHES = N // (P * PAIR)
    MEAN_STEPS = 2
    NORM_STEPS = 2
    SWEEP = RING - 1
    WARM_UP = 6
    DEG_AFTER = 4
    assert STEPS == BANKS

    adj_slots = adj.rearrange("(s j p) (g c) -> g s p j c", p=P, j=PAIR, c=WIDTH)
    x_t_batches = x_t.rearrange("(h p) (m c) -> m p h c", p=P, c=PAIR * P)
    u_t_halves = u_t.rearrange("(h p) k -> p h k", p=P)
    x_last_tiles = x[N - WIDTH:N, :].rearrange("(t p) d -> p t d", p=P)
    x_tiles = x.rearrange("(t p) d -> t p d", p=P)
    out_tiles = out.rearrange("(t p) d -> t p d", p=P)

    ctx = ExitStack()
    with ctx:
        def sbuf(name, shape, dt):
            return ctx.enter_context(nc.sbuf_tensor(name, shape, dt))

        def sem(name):
            return ctx.enter_context(nc.semaphore(name))

        y_parts = sbuf("y_parts", [P, N // P, 2 * D], fp32r)
        adj_raw = [sbuf(f"adj_raw{r}", [P, PAIR, WIDTH], int32) for r in range(RING)]
        adj_f = [sbuf(f"adj_f{r}", [P, PAIR, WIDTH], fp32r) for r in range(RING)]
        deg_part = sbuf("deg_part", [P, WIDTH], fp32r)
        rows = sbuf("rows", [P, BANKS, D], fp32)
        x_t_sb = rows[:, :, :].rearrange("p b d -> p (b d)").rearrange(
            "p (r h c) -> p r h c", r=RING, h=DH)
        x_res = sbuf("x_res", [P, 2, D], fp32)
        u_sb = x_res
        ones = sbuf("ones", [P, 2], fp32r)
        eps = sbuf("eps", [P, 1], fp32)
        rdeg = sbuf("rdeg", [P, BANKS], fp32)
        row_sum = sbuf("row_sum", [P, 2], fp32)
        neg_mean = sbuf("neg_mean", [P, 2], fp32)
        sum_sq = sbuf("sum_sq", [P, 2], fp32)
        std = sbuf("std", [P, 2], fp32)
        rstd = sbuf("rstd", [P, 2], fp32)
        idle = adj_f[RING - 1][:, 0, 0:2 * D]
        x_last = adj_raw[0][:, :, :].bitcast(fp32).rearrange(
            "p j (t d) -> p (j t) d", d=D)
        acc = [ctx.enter_context(nc.psum_tensor(f"acc{b}", [P, 2 * D], fp32)) for b in range(BANKS)]

        idle_cleared = sem("idle_cleared")
        u_loaded = sem("u_loaded")
        x_t_loaded = [sem(f"x_t_loaded{r}") for r in range(RING)]
        y_summed = sem("y_summed")
        y_high_done = sem("y_high_done")
        bank_free = sem("bank_free")
        adj_loaded = [sem(f"adj_loaded{r}") for r in range(RING)]
        adj_converted = sem("adj_converted")
        adj_counted = sem("adj_counted")
        deg_cleared = sem("deg_cleared")
        banks_summed = sem("banks_summed")
        high_copied = sem("high_copied")
        deg_summed = sem("deg_summed")
        rdeg_ready = sem("rdeg_ready")
        consts_ready = sem("consts_ready")
        x_res_loaded = [sem(f"x_res_loaded{k}") for k in range(2)]
        x_last_loaded = sem("x_last_loaded")
        rectified = sem("rectified")
        mean_step = sem("mean_step")
        norm_step = sem("norm_step")
        squares_summed = sem("squares_summed")
        std_ready = sem("std_ready")
        stored = [sem(f"stored{k}") for k in range(2)]

        block = ctx.enter_context(nc.Block())

        @block.gpsimd
        def _(pool):
            nc.gpsimd.memset(ones[:, :].bitcast(fp32), 1.0).then_inc(consts_ready, 1)
            nc.gpsimd.memset(eps[:, :], EPS).then_inc(consts_ready, 1)

        @block.sync
        def _(sp):
            for r in range(RING):
                sp.dma_start(x_t_sb[:, r], x_t_batches[r]).then_inc(x_t_loaded[r], 16)

            def load_x_t(q, r):
                sp.wait_ge(y_summed, q * RING + (r - RING + 1))
                sp.dma_start(x_t_sb[:, r], x_t_batches[q * RING + r]).then_inc(x_t_loaded[r], 16)

            with sp.Fori(1, BATCHES // RING - RING) as q:
                for r in range(RING):
                    load_x_t(q, r)
            for k in range(RING):
                for r in range(RING):
                    load_x_t(BATCHES // RING - RING + k, r)
                sp.dma_start(adj_raw[k][:, :, :], adj_slots[0, k]).then_inc(adj_loaded[k], 16)

            def load_adj(g, s, r):
                n = g * SLOTS + s
                sp.wait_ge(adj_converted, n + (1 - RING))
                sp.wait_ge(adj_counted, PAIR * n + PAIR * (1 - RING))
                sp.dma_start(adj_raw[r][:, :, :], adj_slots[g, s]).then_inc(adj_loaded[r], 16)

            def load_x_res(tile, k):
                sp.dma_start(x_res[:, k], x_tiles[tile]).then_inc(x_res_loaded[k], 16)

            def store(tile, b, k):
                sp.wait_ge(norm_step, NORM_STEPS * tile + NORM_STEPS)
                sp.dma_start(out_tiles[tile], rows[:, b]).then_inc(stored[k], 16)

            sp.wait_ge(y_summed, BATCHES)
            for k in range(2):
                load_x_res(k, k)
            with sp.Fori(0, STEPS - 1) as i:
                for r in range(RING):
                    load_adj(0, i * RING + (RING + r), r)
            for r in range(RING):
                load_adj(1, r, r)

            def group_loads(g, last):
                first_tile = (g - 1) * BANKS

                def finish_tile(b, k, load=True):
                    store(first_tile + b, b, k)
                    if load:
                        load_x_res(first_tile + b + 2, k)

                with sp.Fori(0, STEPS // 2 - 1) as i:
                    for k in range(2):
                        for r in range(RING):
                            load_adj(g, i * (2 * RING) + (k * RING + RING + r), r)
                        finish_tile(i * 2 + k, k)
                for r in range(RING):
                    load_adj(g, (STEPS - 1) * RING + r, r)
                finish_tile(STEPS - 2, 0, not last)
                if not last:
                    for r in range(RING):
                        load_adj(g + 1, r, r)
                else:
                    n = GROUPS * SLOTS - RING
                    sp.wait_ge(adj_converted, n + 1)
                    sp.wait_ge(adj_counted, PAIR * n + PAIR)
                    sp.dma_start(x_last, x_last_tiles).then_inc(x_last_loaded, 16)
                finish_tile(STEPS - 1, 1, not last)

            with sp.Fori(1, GROUPS - 1) as g:
                group_loads(g, False)
            group_loads(LAST, True)

            for b in range(BANKS):
                store(LAST * BANKS + b, b, b % 2)
            for k in range(2):
                sp.wait_ge(stored[k], 16 * GROUPS * BANKS // 2)

        @block.tensor
        def _(pe):
            pe.wait_ge(idle_cleared, 1)
            for _ in range(WARM_UP):
                nc.tensor.matmul(acc[BANKS - 1][:, :], idle[:, 0:P], idle[:, :], start=True, stop=True)
            pe.wait_ge(u_loaded, 16)

            def project(q, r, k, wait_bank):
                pe.wait_ge(x_t_loaded[r], 16 * q + 16)
                if wait_bank:
                    pe.wait_ge(bank_free, q * RING + (r - BANKS + 1))
                for j in range(PAIR):
                    for h in range(DH):
                        done = nc.tensor.matmul(acc[k][:, j * D:(j + 1) * D], x_t_sb[:, r, h, j * P:(j + 1) * P],
                                                u_sb[:, h], start=(h == 0), stop=(h == DH - 1))
                done.then_inc(y_summed, 1)

            for q in range(2):
                for r in range(RING):
                    project(q, r, q * RING + r, False)
            with pe.Fori(1, BATCHES // BANKS) as i:
                for q in range(2):
                    for r in range(RING):
                        project(i * 2 + q, r, q * RING + r, True)

            pe.wait_ge(consts_ready, 2)

            def moving(s, j):
                return y_parts[:, bass.ds(s * PAIR + j, 1), :].rearrange("p o n -> p (o n)")

            def sum_degrees(g):
                pe.wait_ge(adj_counted, g * (SLOTS * PAIR) + SLOTS * PAIR)
                pe.wait_ge(bank_free, g * BANKS + (BATCHES + 1))
                for b in range(BANKS):
                    done = nc.tensor.matmul(acc[0][:, 2 * b:2 * b + 2], deg_part[:, b * P:(b + 1) * P], ones[:, :],
                                            start=True, stop=True, skip_group_check=True)
                done.then_inc(deg_summed, 1)

            def sum_slot(g, s, r, first=False, last=False):
                pe.wait_ge(adj_converted, g * SLOTS + s + 1)
                rhs = [moving(s, j) for j in range(PAIR)]
                for b in ([*range(1, BANKS), 0] if first else range(BANKS)):
                    if first:
                        pe.wait_ge(bank_free, g * BANKS + (BATCHES - BANKS + b + 1))
                        if b == 0:
                            pe.wait_ge(deg_cleared, g + 1)
                    for j in range(PAIR):
                        done = nc.tensor.matmul(acc[b][:, :], adj_f[r][:, j, b * P:(b + 1) * P], rhs[j],
                                                start=(first and j == 0), stop=False, skip_group_check=True)
                    done.then_inc(banks_summed, 1)
                    if last and b == DEG_AFTER:
                        sum_degrees(g)

            def sum_steps(g, steps):
                for r in range(RING):
                    sum_slot(g, r, r, first=(r == 0))
                with pe.Fori(1, steps) as i:
                    for r in range(RING):
                        sum_slot(g, i * RING + r, r)

            with pe.Fori(0, LAST) as g:
                sum_steps(g, STEPS - 1)
                for r in range(RING):
                    sum_slot(g, (STEPS - 1) * RING + r, r, last=(r == RING - 1))
            sum_steps(LAST, STEPS - 1)
            for r in range(RING - SWEEP):
                sum_slot(LAST, (STEPS - 1) * RING + r, r)
            for b in range(BANKS):
                for r in range(RING - SWEEP, RING):
                    s = (STEPS - 1) * RING + r
                    if b == 0:
                        pe.wait_ge(adj_converted, LAST * SLOTS + s + 1)
                    for j in range(PAIR):
                        done = nc.tensor.matmul(acc[b][:, :], adj_f[r][:, j, b * P:(b + 1) * P], moving(s, j),
                                                start=False, stop=(r == RING - 1 and j == PAIR - 1),
                                                skip_group_check=True)
                done.then_inc(banks_summed, 1)
                if b == 1:
                    sum_degrees(LAST)

        @block.scalar
        def _(act):
            act.dma_start(u_sb[:, :, :], u_t_halves).then_inc(u_loaded, 16)

            def write_high(i, k):
                m = i * BANKS + k
                act.wait_ge(y_summed, m + 1)
                high = y_parts[:, bass.ds(m * PAIR, PAIR), 0:D]
                nc.scalar.activation(high, acc[k][:, :].rearrange("p (j d) -> p j d", j=PAIR),
                                     ACT.Copy).then_inc(y_high_done, 1)

            def convert(n, q, r, wait_used=True):
                act.wait_ge(adj_loaded[r], 16 * q + 16)
                if wait_used:
                    act.wait_ge(banks_summed, BANKS * n + BANKS * (1 - RING))
                nc.scalar.activation(adj_f[r][:, :, :], adj_raw[r][:, :, :], ACT.Copy).then_inc(adj_converted, 1)

            def rectify(tile, b):
                act.wait_ge(bank_free, tile + (BATCHES + 1))
                nc.scalar.activation(rows[:, b], rows[:, b], ACT.Relu).then_inc(rectified, 1)

            def find_std(tile, b, k, last_b=None):
                act.wait_ge(mean_step, MEAN_STEPS * tile + MEAN_STEPS)
                one = slice(k, k + 1)
                scratch = x_res[:, k] if last_b is None else x_last[:, last_b]
                nc.scalar.activation(scratch, rows[:, b], ACT.Square, bias=neg_mean[:, one],
                                     accum_out=sum_sq[:, one]).then_inc(squares_summed, 1)
                act.wait_ge(squares_summed, tile + 1)
                nc.scalar.activation(std[:, one], sum_sq[:, one], ACT.Sqrt, bias=eps[:, :],
                                     scale=1.0 / D).then_inc(std_ready, 1)

            def convert_step(g, i, k=None):
                q = g * STEPS + i
                convert(q * RING + 2, q, 2)
                convert(q * RING + 3, q, 3)
                if k is not None:
                    find_std((g - 1) * BANKS + i, bass.ds(i, 1), k)
                convert(q * RING + 4, q + 1, 0)
                convert(q * RING + 5, q + 1, 1)

            def copy_high_half(g, before, b):
                if g is not None and b < 2:
                    act.wait_ge(stored[b], g * (16 * BANKS // 2))
                act.wait_ge(banks_summed, before + (b + 1))
                nc.scalar.activation(rows[:, b], acc[b][:, 0:D], ACT.Copy).then_inc(high_copied, 1)

            def fill_rows(g, wait_stored=True):
                for b in range(BANKS + 1):
                    if b < BANKS:
                        copy_high_half(g if wait_stored else None, g * (SLOTS * BANKS) + (SLOTS - 1) * BANKS, b)
                    if b >= 1:
                        rectify(g * BANKS + b - 1, slice(b - 1, b))

            with act.Fori(0, BATCHES // BANKS - 1) as i:
                for k in range(BANKS):
                    write_high(i, k)
            act.wait_ge(consts_ready, 2)
            for k in range(BANKS):
                write_high(BATCHES // BANKS - 1, k)
                if k == 2:
                    convert(0, 0, 0, False)
                if k == 5:
                    convert(1, 0, 1, False)
            convert(2, 0, 2, False)
            convert(3, 0, 3, False)
            convert(4, 1, 0)
            convert(5, 1, 1)
            with act.Fori(1, STEPS) as i:
                convert_step(0, i)
            fill_rows(0, False)
            with act.Fori(1, GROUPS - 1) as g:
                with act.Fori(0, STEPS // 2) as i:
                    for k in range(2):
                        convert_step(g, i * 2 + k, k)
                fill_rows(g)
            with act.Fori(0, STEPS // 2 - 1) as i:
                for k in range(2):
                    convert_step(LAST, i * 2 + k, k)
            convert_step(LAST, STEPS - 2, 0)
            q = GROUPS * STEPS - 1
            convert(q * RING + 2, q, 2)
            convert(q * RING + 3, q, 3)
            find_std(LAST * BANKS - 1, slice(BANKS - 1, BANKS), 1)
            for b in range(BANKS + 2):
                if b < BANKS:
                    copy_high_half(LAST, (GROUPS * SLOTS - SWEEP) * BANKS, b)
                if 0 <= b - 1 < BANKS:
                    rectify(LAST * BANKS + b - 1, slice(b - 1, b))
                if 0 <= b - 2:
                    find_std(LAST * BANKS + b - 2, slice(b - 2, b - 1), b % 2, b - 2)

        @block.vector
        def _(dve):
            nc.vector.memset(idle.bitcast(fp32), 0.0).then_inc(idle_cleared, 1)
            with dve.Fori(0, BATCHES // BANKS) as i:
                for k in range(BANKS):
                    m = i * BANKS + k
                    dve.wait_ge(y_high_done, m + 1)
                    high = y_parts[:, bass.ds(m * PAIR, PAIR), 0:D].bitcast(fp32)
                    low = y_parts[:, bass.ds(m * PAIR, PAIR), D:2 * D]
                    nc.vector.tensor_tensor(low, acc[k][:, :].rearrange("p (j d) -> p j d", j=PAIR), high,
                                            ALU.subtract).then_inc(bank_free, 1)

            def clear_deg(g):
                nc.vector.memset(deg_part[:, :].bitcast(fp32), 0.0).then_inc(deg_cleared, 1)

            def count_slot(n, q, r, g=None, first=False):
                if g is not None:
                    dve.wait_ge(deg_cleared, g + 1)
                dve.wait_ge(adj_loaded[r], 16 * q + 16)
                for j in range(PAIR):
                    if not first or r or j:
                        dve.wait_ge(adj_counted, n * PAIR + j)
                    nc.vector.tensor_tensor(deg_part[:, :], deg_part[:, :].bitcast(fp32), adj_raw[r][:, j],
                                            ALU.add).then_inc(adj_counted, 1)

            def scale_and_add_x(tile, b, k, g, x_tile):
                dve.wait_ge(rdeg_ready, g + 1)
                dve.wait_ge(rectified, tile + 1)
                nc.vector.scalar_tensor_tensor(rows[:, b], rows[:, b], rdeg[:, b], x_tile, ALU.mult, ALU.add,
                                               accum_out=row_sum[:, k:k + 1]).then_inc(mean_step, 1)

            def find_neg_mean(tile, k):
                dve.wait_ge(mean_step, MEAN_STEPS * tile + 1)
                nc.vector.tensor_scalar(neg_mean[:, k:k + 1], row_sum[:, k:k + 1], -1.0 / D, None,
                                        ALU.mult).then_inc(mean_step, 1)

            def invert_std(tile, k):
                dve.wait_ge(std_ready, tile + 1)
                nc.vector.reciprocal(rstd[:, k:k + 1], std[:, k:k + 1]).then_inc(norm_step, 1)

            def normalise(tile, b, k):
                dve.wait_ge(norm_step, NORM_STEPS * tile + 1)
                nc.vector.tensor_scalar(rows[:, b], rows[:, b], neg_mean[:, k:k + 1], rstd[:, k:k + 1],
                                        ALU.add, ALU.mult).then_inc(norm_step, 1)

            def add_low_half(g, b):
                dve.wait_ge(high_copied, g * BANKS + (b + 1))
                nc.vector.tensor_tensor(rows[:, b], acc[b][:, D:2 * D], rows[:, b], ALU.add).then_inc(bank_free, 1)

            def invert_degrees(g):
                dve.wait_ge(deg_summed, g + 1)
                nc.vector.reciprocal(rdeg[:, :], acc[0][:, 0:2 * BANKS:2]).then_inc(rdeg_ready, 1)

            def empty_banks(g):
                for b in range(BANKS):
                    add_low_half(g, b)
                    if b == DEG_AFTER + 1:
                        invert_degrees(g)

            clear_deg(0)
            for r in range(RING):
                count_slot(r, 0, r, 0 if r == 0 else None, first=True)
            with dve.Fori(1, STEPS) as i:
                for r in range(RING):
                    count_slot(i * RING + r, i, r, 0 if r == 0 else None)
            empty_banks(0)

            def group(g):
                clear_deg(g)
                with dve.Fori(0, STEPS // 2) as i:
                    for k in range(2):
                        q = g * STEPS + i * 2 + k
                        b = bass.ds(i * 2 + k, 1)
                        tile = (g - 1) * BANKS + i * 2 + k
                        count_slot(q * RING, q, 0, g)
                        dve.wait_ge(x_res_loaded[k], (g - 1) * (16 * BANKS // 2) + (i * 16 + 16))
                        scale_and_add_x(tile, b, k, g - 1, x_res[:, k:k + 1])
                        count_slot(q * RING + 1, q, 1)
                        find_neg_mean(tile, k)
                        count_slot(q * RING + 2, q, 2)
                        count_slot(q * RING + 3, q, 3)
                        invert_std(tile, k)
                        normalise(tile, b, k)

            with dve.Fori(1, LAST) as g:
                group(g)
                empty_banks(g)
            group(LAST)

            first = LAST * BANKS
            add_low_half(LAST, 0)
            for b in range(1, BANKS + 2):
                if b < BANKS:
                    add_low_half(LAST, b)
                if b == 1:
                    invert_degrees(LAST)
                    dve.wait_ge(x_last_loaded, 16)
                if b - 1 < BANKS:
                    scale_and_add_x(first + b - 1, slice(b - 1, b), (b - 1) % 2, LAST, x_last[:, b - 1:b])
                if b >= 2:
                    invert_std(first + b - 2, b % 2)
                if b - 1 < BANKS:
                    find_neg_mean(first + b - 1, (b - 1) % 2)
                if b >= 2:
                    normalise(first + b - 2, slice(b - 2, b - 1), b % 2)


def kernel(x, adj, L0_gnn_U):
    import numpy as np
    import concourse.bacc as bacc
    from concourse.bass_utils import run_bass_kernel_spmd

    x, adj, u = np.asarray(x), np.asarray(adj), np.asarray(L0_gnn_U)
    arrays = {
        "x": np.ascontiguousarray(x),
        "x_t": np.ascontiguousarray(x.T),
        "adj": np.ascontiguousarray(adj),
        "u_t": np.ascontiguousarray(u.T),
    }
    nc = bacc.Bacc("TRN2", target_bir_lowering=False, num_devices=1)
    args = [nc.dram_tensor(name, a.shape, mybir.dt.from_np(a.dtype), kind="ExternalInput").ap()
            for name, a in arrays.items()]
    out = nc.dram_tensor("out", x.shape, mybir.dt.float32, kind="ExternalOutput").ap()
    build_graph_norm(nc, *args, out)
    return run_bass_kernel_spmd(nc, [arrays], core_ids=[0]).results[0]["out"]
```
